# Optimizing a Trainium2 kernel written in Bass

```python
import numpy as np
import jax
import jax.numpy as jnp

def _softmax(x, axis=-1):
    return jax.nn.softmax(x, axis=axis)

def _gelu(x):
    return jax.nn.gelu(x, approximate=True)

def _silu(x):
    return jax.nn.silu(x)

def _sigmoid(x):
    return jax.nn.sigmoid(x)

def _layernorm(x, axis=-1, eps=1e-05):
    m = jnp.mean(x, axis=axis, keepdims=True)
    v = jnp.var(x, axis=axis, keepdims=True)
    return (x - m) / jnp.sqrt(v + eps)

def _scatter_add(tgt, idx, src, axis=0):
    return tgt.at[idx].add(src)

def _segment_sum(src, seg, n):
    return jax.ops.segment_sum(src, seg, n)
kernel_name = 'mk_gnn_resnorm_d4_gnn_r32_26bd64'

def setup_inputs(seed: int=0):
    np.random.seed(seed)
    _w = jnp.asarray

    def _rec_inputs():
        import jax
        import jax.numpy as jnp
        _gk = jax.random.key(seed)
        x = -0.000202 + 1 * jax.random.normal(jax.random.fold_in(_gk, 1), (3125, 128), jnp.float32)
        src = jax.random.randint(jax.random.fold_in(_gk, 2), (100000,), 0, 3125, jnp.int32)
        dst = jnp.minimum((3125 * jax.random.uniform(jax.random.fold_in(_gk, 3), (100000,)) ** 2.0).astype(jnp.int32), 99999)
        _o = jnp.argsort(dst, stable=True)
        src = src[_o]
        dst = dst[_o]
        edge_attr_4 = -0.000203651 + 1.0002 * jax.random.normal(jax.random.fold_in(_gk, 13), (100000, 4), jnp.float32)
        edge_type_8 = jax.random.randint(jax.random.fold_in(_gk, 15), (100000,), 0, 8, jnp.int32)
        return (x, src, dst, edge_attr_4, edge_type_8)
    x, src, dst, edge_attr_4, edge_type_8 = _rec_inputs()

    def _L0_gnn_setup():
        import jax, jax.numpy as jnp
        import numpy as np
        N_NODES = 50000
        N_EDGES = 18750
        F_IN = 128
        F_OUT = 128
        N_RELS = 8
        key = jax.random.key(seed)
        k1, k2, k3, k4, k5 = jax.random.split(key, 5)
        X = jax.random.normal(k1, (N_NODES, F_IN), dtype=jnp.float32)
        W = jax.random.normal(k2, (N_RELS, F_OUT, F_IN), dtype=jnp.float32) * (1.0 / np.sqrt(F_IN))
        edge_src = jax.random.randint(k3, (N_EDGES,), 0, N_NODES, dtype=jnp.int32)
        edge_dst = jax.random.randint(k4, (N_EDGES,), 0, N_NODES, dtype=jnp.int32)
        edge_type = jax.random.randint(k5, (N_EDGES,), 0, N_RELS, dtype=jnp.int32)
        return {'X': X, 'W': W, 'edge_src': edge_src, 'edge_dst': edge_dst, 'edge_type': edge_type, 'num_nodes': N_NODES}
    _L0_gnn_all = _L0_gnn_setup()
    _L0_gnn_in = {k: v for k, v in _L0_gnn_all.items() if k in ('W',)}
    del _L0_gnn_all

    def _L1_gnn_setup():
        import jax, jax.numpy as jnp
        import numpy as np
        N_NODES = 50000
        N_EDGES = 25000
        D_FEAT = 128
        D_OUT = 128
        key = jax.random.key(seed)
        k1, k2, k3, k4 = jax.random.split(key, 4)
        x = jax.random.normal(k1, (N_NODES, D_FEAT), dtype=jnp.float32)
        edge_index = jax.random.randint(k2, (2, N_EDGES), 0, N_NODES, dtype=jnp.int64)
        W = jax.random.normal(k3, (D_OUT, 2 * D_FEAT), dtype=jnp.float32) * (1.0 / np.sqrt(2 * D_FEAT))
        b = jax.random.normal(k4, (D_OUT,), dtype=jnp.float32) * 0.01
        return {'x': x, 'edge_index': edge_index, 'W': W, 'b': b}
    _L1_gnn_all = _L1_gnn_setup()
    _L1_gnn_in = {k: v for k, v in _L1_gnn_all.items() if k in ('W', 'b')}
    del _L1_gnn_all

    def _L2_gnn_setup():
        import jax, jax.numpy as jnp
        import numpy as np
        N_NODES = 10000
        N_EDGES = 20000
        D_IN = 128
        D_OUT = 128
        EDGE_DIM = 4
        LN_EPS = 1e-05
        NEG_SLOPE = 0.01
        key = jax.random.key(seed)
        ks = jax.random.split(key, 6)
        x = jax.random.normal(ks[0], (N_NODES, D_IN), dtype=jnp.float32)
        edge_attr = jax.random.normal(ks[1], (N_EDGES, EDGE_DIM), dtype=jnp.float32)
        limit = float(np.sqrt(6.0 / (D_IN + D_OUT)))
        W = jax.random.uniform(ks[2], (D_OUT, D_IN), minval=-limit, maxval=limit, dtype=jnp.float32)
        b = jnp.zeros((D_OUT,), dtype=jnp.float32)
        gamma = jnp.ones((D_OUT,), dtype=jnp.float32)
        beta = jnp.zeros((D_OUT,), dtype=jnp.float32)
        edge_index = jax.random.randint(ks[3], (2, N_EDGES), 0, N_NODES, dtype=jnp.int64)
        return {'x': x, 'edge_attr': edge_attr, 'W': W, 'b': b, 'gamma': gamma, 'beta': beta, 'edge_index': edge_index}
    _L2_gnn_all = _L2_gnn_setup()
    _L2_gnn_in = {k: v for k, v in _L2_gnn_all.items() if k in ('W', 'b', 'gamma', 'beta')}
    del _L2_gnn_all

    def _L3_gnn_setup():
        import jax, jax.numpy as jnp
        import numpy as np
        N_NODES = 3125
        N_EDGES = 100000
        FEAT = 128
        K = 4

        def spmm(x, edge_index, deg_inv_sqrt, num_nodes):
            src, dst = (edge_index[0], edge_index[1])
            norm = deg_inv_sqrt[src] * deg_inv_sqrt[dst]
            msg = x[src] * norm[:, None]
            return jax.ops.segment_sum(msg, dst, num_segments=num_nodes)
        key = jax.random.key(seed)
        k1, k2, k3, k4 = jax.random.split(key, 4)
        x = jax.random.normal(k1, (N_NODES, FEAT), dtype=jnp.float32)
        edge_index_with_loops = jax.random.randint(k2, (2, N_EDGES), 0, N_NODES, dtype=jnp.int32)
        deg_inv_sqrt = jax.random.uniform(k3, (N_NODES,), dtype=jnp.float32)
        weights = jax.random.normal(k4, (K, FEAT, FEAT), dtype=jnp.float32) * 0.01
        return {'x': x, 'edge_index_with_loops': edge_index_with_loops, 'deg_inv_sqrt': deg_inv_sqrt, 'num_nodes': N_NODES, 'weights': weights}
    _L3_gnn_all = _L3_gnn_setup()
    _L3_gnn_in = {k: v for k, v in _L3_gnn_all.items() if k in ('weights',)}
    del _L3_gnn_all
    return {'x': x, 'src': src, 'dst': dst, 'edge_attr_4': edge_attr_4, 'edge_type_8': edge_type_8, 'L0_gnn_W': _L0_gnn_in['W'], 'L1_gnn_W': _L1_gnn_in['W'], 'L1_gnn_b': _L1_gnn_in['b'], 'L2_gnn_W': _L2_gnn_in['W'], 'L2_gnn_b': _L2_gnn_in['b'], 'L2_gnn_gamma': _L2_gnn_in['gamma'], 'L2_gnn_beta': _L2_gnn_in['beta'], 'L3_gnn_weights': _L3_gnn_in['weights']}

def reference(x, src, dst, edge_attr_4, edge_type_8, L0_gnn_W, L1_gnn_W, L1_gnn_b, L2_gnn_W, L2_gnn_b, L2_gnn_gamma, L2_gnn_beta, L3_gnn_weights):
    import jax
    import jax.numpy as jnp

    def _L0_gnn_ref(X, W, edge_src, edge_dst, edge_type, num_nodes):
        import jax, jax.numpy as jnp
        import numpy as np
        N_NODES = 50000
        N_EDGES = 18750
        F_IN = 128
        F_OUT = 128
        N_RELS = 8
        H = jnp.einsum('nf,rof->rno', X, W)
        msgs = H[edge_type, edge_src]
        Y = jax.ops.segment_sum(msgs, edge_dst, num_segments=num_nodes)
        return Y

    def _L1_gnn_ref(x, edge_index, W, b):
        import jax, jax.numpy as jnp
        import numpy as np
        N_NODES = 50000
        N_EDGES = 25000
        D_FEAT = 128
        D_OUT = 128
        src, dst = (edge_index[0], edge_index[1])
        agg = jax.ops.segment_sum(x[src], dst, num_segments=x.shape[0])
        h = jnp.concatenate([x, agg], axis=1)
        h = h @ W.T + b
        return jax.nn.relu(h)

    def _L2_gnn_ref(x, edge_attr, W, b, gamma, beta, edge_index):
        import jax, jax.numpy as jnp
        import numpy as np
        N_NODES = 10000
        N_EDGES = 20000
        D_IN = 128
        D_OUT = 128
        EDGE_DIM = 4
        LN_EPS = 1e-05
        NEG_SLOPE = 0.01
        N = x.shape[0]
        ew = jnp.abs(edge_attr[:, 0])
        loop = jnp.arange(N, dtype=edge_index.dtype)
        row = jnp.concatenate([edge_index[0], loop])
        col = jnp.concatenate([edge_index[1], loop])
        w = jnp.concatenate([ew, jnp.ones((N,), dtype=x.dtype)])
        deg = jax.ops.segment_sum(w, col, num_segments=N)
        dinv = jnp.where(deg > 0, jax.lax.rsqrt(deg), 0.0)
        norm = dinv[row] * w * dinv[col]
        h = x @ W.T + b
        msg = h[row] * norm[:, None]
        out = jax.ops.segment_sum(msg, col, num_segments=N)
        out = jnp.where(out >= 0, out, NEG_SLOPE * out)
        mu = jnp.mean(out, axis=-1, keepdims=True)
        var = jnp.mean(jnp.square(out - mu), axis=-1, keepdims=True)
        out = (out - mu) * jax.lax.rsqrt(var + LN_EPS) * gamma + beta
        return out

    def _L3_gnn_ref(x, edge_index_with_loops, deg_inv_sqrt, num_nodes, weights):
        import jax, jax.numpy as jnp
        import numpy as np
        N_NODES = 3125
        N_EDGES = 100000
        FEAT = 128
        K = 4

        def spmm(x, edge_index, deg_inv_sqrt, num_nodes):
            src, dst = (edge_index[0], edge_index[1])
            norm = deg_inv_sqrt[src] * deg_inv_sqrt[dst]
            msg = x[src] * norm[:, None]
            return jax.ops.segment_sum(msg, dst, num_segments=num_nodes)
        Kk = weights.shape[0]
        T = [x]
        if Kk > 1:
            T.append(spmm(x, edge_index_with_loops, deg_inv_sqrt, num_nodes))
        for k in range(2, Kk):
            T.append(2.0 * spmm(T[k - 1], edge_index_with_loops, deg_inv_sqrt, num_nodes) - T[k - 2])
        Ts = jnp.stack(T, axis=0)
        return jnp.einsum('knf,kfo->no', Ts, weights)
    edge_index = jnp.stack([src, dst])
    deg = jnp.maximum(jax.ops.segment_sum(jnp.ones(dst.shape, jnp.float32), dst, num_segments=3125), 1.0)
    deg_isqrt = deg ** (-0.5)
    x = _layernorm(x + _L0_gnn_ref(x, L0_gnn_W, src, dst, edge_type_8, 3125), axis=-1)
    x = _layernorm(x + _L1_gnn_ref(x, edge_index, L1_gnn_W, L1_gnn_b), axis=-1)
    x = _layernorm(x + _L2_gnn_ref(x, edge_attr_4, L2_gnn_W, L2_gnn_b, L2_gnn_gamma, L2_gnn_beta, edge_index), axis=-1)
    x = _layernorm(x + _L3_gnn_ref(x, edge_index, deg_isqrt, 3125, L3_gnn_weights), axis=-1)
    return x

_drawn_inputs = setup_inputs


def setup_inputs(seed=0):
    import zlib

    import numpy as np

    out = dict(_drawn_inputs(seed))
    spreads = {'L2_gnn_b': (0.0, 0.1), 'L2_gnn_gamma': (1.0, 0.2), 'L2_gnn_beta': (0.0, 0.1)}
    factors = {'L1_gnn_b': 8.0}
    for name, (base, spread) in spreads.items():
        noise = np.random.default_rng([zlib.crc32(name.encode()), seed]).standard_normal(out[name].shape)
        drawn = base * np.exp(spread * noise) if base else spread * noise
        out[name] = jnp.asarray(drawn.astype(out[name].dtype))
    for name, factor in factors.items():
        out[name] = (out[name] * factor).astype(out[name].dtype)
    return out
```

```python
from contextlib import ExitStack

import concourse.bass as bass
from concourse import mybir

P = 128
NODES, EDGES, FEAT, RELS, CHEB = 3125, 100000, 128, 8, 4
BLOCKS = -(-NODES // P)
NPAD = BLOCKS * P
TAIL = NODES - (BLOCKS - 1) * P
FULL_TILES = EDGES // P
GROUPS, GROUP = 7, 112
EDGE_TILES = GROUPS * GROUP
WIN = 16
WINDOWS = NPAD // WIN
SLOT = BLOCKS * WIN
RCOL = RELS * WIN
QUARTER = 32
QUARTERS = NPAD // QUARTER
ITEM = SLOT + RCOL + 4 * P
ITEMS, GSLOTS = 4, 8
NOWHERE = 4088
EPS = 1e-5
SLOPE = 0.01


def gnn_kernel(nc, x, src, dst, edge_attr, edge_type, W_rel, W_sum, b_sum, W_deg, b_deg, gamma, beta,
               W_cheb, out):
    f32, bf16, i32, u16 = mybir.dt.float32, mybir.dt.bfloat16, mybir.dt.int32, mybir.dt.uint16
    ALU, ACT, AX = mybir.AluOpType, mybir.ActivationFunctionType, mybir.AxisListType
    ds = bass.ds
    with ExitStack() as ctx:
        def sem(name):
            return ctx.enter_context(nc.semaphore(name))

        x_pieces = nc.dram_tensor("x_pieces", [NPAD, 3 * FEAT], bf16).ap()
        wadj = nc.dram_tensor("wadj", [QUARTERS, P, BLOCKS * QUARTER], f32).ap()
        rel_out = nc.dram_tensor("rel_out", [NPAD, FEAT + 1], f32).ap()
        count_d = nc.dram_tensor("count_d", [1, WINDOWS], f32).ap()
        weights_t = nc.dram_tensor("weights_t", [FEAT, 3 * FEAT], f32).ap()
        u_pieces = nc.dram_tensor("u_pieces", [NPAD, 3 * FEAT], bf16).ap()
        cheb_prev = nc.dram_tensor("cheb_prev", [2, NPAD, FEAT], f32).ap()
        cheb_sum = nc.dram_tensor("cheb_sum", [NPAD, FEAT], f32).ap()

        ADJ_BYTES = BLOCKS * NPAD * 2
        WORK_BYTES = 52800
        adj_mem = ctx.enter_context(nc.sbuf_tensor("adj_mem", [P, ADJ_BYTES // 2], bf16))
        work_mem = ctx.enter_context(nc.sbuf_tensor("work_mem", [P, WORK_BYTES // 2], bf16))
        adj = adj_mem[:, :].rearrange("p (h n) -> p h n", h=BLOCKS)
        psum = ctx.enter_context(nc.psum_tensor("psum", [P, 8, 512], f32))

        def cutter(mem, start, end):
            at = [start]

            def cut(shape, dt):
                n = 1
                for s in shape:
                    n *= s
                size = n if dt in (bf16, u16) else 2 * n
                v = mem[:, at[0]:at[0] + size]
                at[0] += size + size % 2
                assert at[0] * 2 <= end, (at[0] * 2, end)
                v = v if dt == bf16 else v.bitcast(dt)
                if len(shape) == 2:
                    v = v.rearrange("p (a b) -> p a b", a=shape[0])
                if len(shape) == 3:
                    v = v.rearrange("p (a b c) -> p a b c", a=shape[0], b=shape[1])
                return v
            return cut

        cut = cutter(work_mem, 0, WORK_BYTES)
        wstage = cut([2, BLOCKS, QUARTER], f32)
        rel_sum = cut([RELS, P], f32)
        deg_sum = cut([RELS, P], f32)
        slot_key = cut([EDGE_TILES + 1], u16)
        rel_key = cut([EDGE_TILES + 1], u16)
        win_key = cut([EDGE_TILES + 1], u16)
        in_window = cut([EDGE_TILES + 1], u16)
        lane_key = cut([EDGE_TILES + 1], bf16)
        w_piece = cut([EDGE_TILES + 1, 3], bf16)
        src_idx = cut([EDGE_TILES], i32)
        idx_now = cut([2, GSLOTS], i32)
        walk = cut([WINDOWS + 1], i32)
        iota_slot = cut([SLOT], u16)
        ring = cut([ITEMS, ITEM], bf16)
        grows = cut([GSLOTS, 3 * FEAT], bf16)
        WrelT = cut([RELS, FEAT], f32)
        rel_row = cut([FEAT + 1], f32)
        ones_col = cut([1], f32)
        iota_rel, iota_lane, iota_win = iota_slot[:, 0:RCOL], iota_slot[:, 0:P], iota_slot[:, 0:WINDOWS]

        pcut = cutter(adj_mem, 0, ADJ_BYTES)
        dst_i, src_i, typ_i = (pcut([GROUPS, P], i32) for _ in range(3))
        key_i = [pcut([GROUPS, P], i32) for _ in range(4)]
        tmp_i = pcut([GROUPS, P], i32)
        attr = pcut([GROUPS, 4 * P], f32)
        NFIELD = 7
        field = [pcut([GROUPS, P], f32) for _ in range(NFIELD)]
        x_nat = pcut([BLOCKS, FEAT], f32)
        x_rest = pcut([BLOCKS, FEAT], f32)
        x3 = pcut([BLOCKS, 3 * FEAT], bf16)
        W_nat = pcut([RELS + 3, FEAT], f32)
        W_t = pcut([3, FEAT], f32)
        ident0 = pcut([P], f32)
        ones = pcut([P], f32)
        w_all = pcut([EDGE_TILES], f32)
        w_rest = pcut([EDGE_TILES], f32)
        first_dst = pcut([EDGE_TILES], f32)
        first_all = pcut([EDGE_TILES], f32)
        SPAN = (EDGES - 1) // P
        REACH = EDGES - 1 - (P - 1) * SPAN
        pair = pcut([REACH + 1], i32)
        unsorted_at = pcut([REACH], f32)
        small = pcut([16], f32)
        row = pcut([4, WINDOWS], f32)

        loaded_edges, loaded_x, loaded_w, loaded_pair = sem("loaded_edges"), sem("loaded_x"), sem("loaded_w"), sem("loaded_pair")
        zeroed = sem("zeroed")
        pool_made, fields_made, field_t, field_out = sem("pool_made"), sem("fields_made"), sem("field_t"), sem("field_out")
        wt_done, wt_out, wt_stored = sem("wt_done"), sem("wt_out"), sem("wt_stored")
        x_split, x_stored = sem("x_split"), sem("x_stored")
        dve_step, flag_sum = sem("dve_step"), sem("flag_sum")
        first_row, first_bc = sem("first_row"), sem("first_bc")
        counts_made, counts_in, counts_out = sem("counts_made"), sem("counts_in"), sem("counts_out")
        tables_ready = sem("tables_ready")
        masked = sem("masked")
        onehots_ready, items_done = sem("onehots_ready"), sem("items_done")
        landed = [sem(f"landed{i}") for i in range(GSLOTS)]
        idx_copied = sem("idx_copied")
        rows_ready, rows_free = sem("rows_ready"), sem("rows_free")
        acc_free = sem("acc_free")
        wadj_stored = [sem(f"wadj_stored{i}") for i in range(2)]
        rel_ready, rel_stored = sem("rel_ready"), sem("rel_stored")
        rel_evac = sem("rel_evac")

        ACC, WACC, RACC, BLK = range(4)

        block = nc.Block()
        block.__enter__()

        def rows_of(t):
            return t[0:FULL_TILES * P].rearrange("(t e) -> t e", e=P)

        @block.sync
        def _(sp):
            sp.wait_ge(zeroed, 1)
            for t, to in ((dst, dst_i), (src, src_i), (edge_type, typ_i)):
                r = rows_of(t)
                full = (GROUPS - 1) * GROUP
                sp.dma_start(to[0:GROUP, 0:GROUPS - 1, :], r[0:full, :].rearrange("(g t) e -> t g e", t=GROUP)).then_inc(loaded_edges, 16)
                last = FULL_TILES - full
                sp.dma_start(to[0:last, GROUPS - 1, :], r[full:FULL_TILES, :]).then_inc(loaded_edges, 16)
                sp.dma_start(to[last:last + 1, GROUPS - 1, 0:EDGES - FULL_TILES * P],
                             t[FULL_TILES * P:EDGES].rearrange("(o e) -> o e", o=1)).then_inc(loaded_edges, 16)
            r = edge_attr[0:FULL_TILES * P, :].rearrange("(t e) c -> t (e c)", e=P)
            sp.dma_start(attr[0:GROUP, 0:GROUPS - 1, :], r[0:full, :].rearrange("(g t) e -> t g e", t=GROUP)).then_inc(loaded_edges, 16)
            sp.dma_start(attr[0:last, GROUPS - 1, :], r[full:FULL_TILES, :]).then_inc(loaded_edges, 16)
            n = EDGES - FULL_TILES * P
            sp.dma_start(attr[last:last + 1, GROUPS - 1, 0:4 * n],
                         edge_attr[FULL_TILES * P:EDGES, :].rearrange("(o e) c -> o (e c)", o=1)).then_inc(loaded_edges, 16)
            sp.wait_ge(x_split, 1)
            sp.dma_start(x_pieces.rearrange("(h p) c -> p h c", p=P), x3).then_inc(x_stored, 16)
            sp.wait_ge(counts_made, 1)
            sp.dma_start(count_d.rearrange("o (p j) -> (o p) j", j=2), small[0:WINDOWS // 2, 4:6]).then_inc(counts_in, 16)
            sp.wait_ge(counts_in, 16)
            sp.dma_start(row[0:1, 0, :], count_d).then_inc(counts_out, 16)
            sp.wait_ge(wt_out, 2)
            sp.dma_start(weights_t, W_t.rearrange("p a b -> p (a b)")).then_inc(wt_stored, 16)
            sp.wait_ge(wt_stored, 16)
            sp.wait_ge(tables_ready, 1)
            back = sp.value_load(walk[0:1, WINDOWS:WINDOWS + 1], min_val=0, max_val=EDGE_TILES)
            passes = sp.snap(back * (WINDOWS - 1) // EDGE_TILES + 1, min_val=1, max_val=WINDOWS)
            with sp.Fori(0, passes) as ps:
                with sp.Fori(0, EDGE_TILES // GSLOTS) as k:
                    turn = sp.snap(ps * (EDGE_TILES // GSLOTS) + k)
                    for s in range(GSLOTS):
                        sp.wait_ge(landed[s], turn * 16 + 16)
                        sp.sem_inc(rows_ready, 1)

        @block.gpsimd
        def _(pool):
            nc.gpsimd.memset(ones, 1.0).then_inc(pool_made, 1)
            nc.gpsimd.iota(iota_slot, pattern=[[1, SLOT]], base=0, channel_multiplier=0).then_inc(pool_made, 1)
            nc.gpsimd.iota(small[:, 0:2], pattern=[[WIN, 2]], base=WIN - 1, channel_multiplier=2 * WIN,
                           allow_small_or_imprecise_dtypes=True).then_inc(pool_made, 1)
            nc.gpsimd.iota(row[0:1, 3, :], pattern=[[EDGE_TILES, WINDOWS]], base=EDGE_TILES, channel_multiplier=0,
                           allow_small_or_imprecise_dtypes=True).then_inc(pool_made, 1)
            pool.wait_ge(pool_made, 1)
            nc.gpsimd.affine_select(out=ident0, in_=ones, compare_op=ALU.is_equal, fill=0.0, base=0,
                                    pattern=[[-1, P]], channel_multiplier=1).then_inc(pool_made, 1)
            pool.wait_ge(tables_ready, 1)
            pool.wait_ge(x_stored, 16)
            back = pool.value_load(walk[0:1, WINDOWS:WINDOWS + 1], min_val=0, max_val=EDGE_TILES)
            passes = pool.snap(back * (WINDOWS - 1) // EDGE_TILES + 1, min_val=1, max_val=WINDOWS)
            issued = pool.alloc_register("issued")
            pool.reg_mov(issued, 0)
            with pool.Fori(0, passes) as ps:
                with pool.Fori(0, EDGE_TILES // (2 * GSLOTS)) as k:
                    turn = pool.snap(ps * (EDGE_TILES // (2 * GSLOTS)) + k)
                    for h in range(2):
                        nc.gpsimd.tensor_copy(idx_now[:, h, :], src_idx[:, ds((k * 2 + h) * GSLOTS, GSLOTS)]).then_inc(idx_copied, 1)
                        pool.wait_ge(idx_copied, turn * 2 + (h + 1))
                        for s in range(GSLOTS):
                            pool.wait_ge(rows_free, pool.snap(issued) + 1)
                            pool.reg_add(issued, issued, 1)
                            nc.gpsimd.indirect_dma_start(
                                out=grows[:, s, :], out_offset=None, in_=x_pieces,
                                in_offset=bass.IndirectOffsetOnAxis(ap=idx_now[:, h, s:s + 1], axis=0),
                            ).then_inc(landed[s], 16)

        @block.vector
        def _(dve):
            count = [0]

            def link(ins):
                count[0] += 1
                ins.then_inc(dve_step, 1)
                dve.wait_ge(dve_step, count[0])

            v = nc.vector
            for t in (src_i, typ_i, attr):
                v.memset(t, 0)
            v.memset(x_nat[:, BLOCKS - 1, :], 0.0)
            link(v.memset(dst_i, NOWHERE))
            v.memset(small[:, 2:3], 0.0).then_inc(zeroed, 1)

            dve.wait_ge(loaded_x, 32)
            link(v.tensor_copy(x3[:, :, 0:FEAT], x_nat))
            link(v.tensor_tensor(x_rest, x_nat, x3[:, :, 0:FEAT], ALU.subtract))
            link(v.tensor_copy(x3[:, :, FEAT:2 * FEAT], x_rest))
            v.tensor_tensor(x3[:, :, 2 * FEAT:], x_rest, x3[:, :, FEAT:2 * FEAT], ALU.subtract).then_inc(x_split, 1)

            dve.wait_ge(loaded_edges, 12 * 16)
            G = slice(0, GROUP)
            slot_i, lane_i, rel_i, win_i = key_i
            link(v.tensor_scalar(tmp_i[G], dst_i[G], WIN - 1, None, ALU.bitwise_and))
            v.tensor_scalar(lane_i[G], src_i[G], P - 1, None, ALU.bitwise_and)
            v.tensor_scalar(win_i[G], dst_i[G], 4, None, ALU.arith_shift_right)
            v.tensor_scalar(rel_i[G], typ_i[G], 4, None, ALU.logical_shift_left)
            link(v.tensor_scalar(slot_i[G], src_i[G], 7, 4, ALU.arith_shift_right, ALU.logical_shift_left))
            v.tensor_tensor(slot_i[G], slot_i[G], tmp_i[G], ALU.bitwise_or)
            link(v.tensor_tensor(rel_i[G], rel_i[G], tmp_i[G], ALU.bitwise_or))
            for f, t in enumerate((slot_i, lane_i, rel_i, win_i, src_i)):
                v.tensor_copy(field[f][G], t[G]).then_inc(fields_made, 1)
            av = attr[G].rearrange("p g (e c) -> p g e c", c=4)[:, :, :, 0]
            v.scalar_tensor_tensor(field[5][G], av, -1.0, av, ALU.mult, ALU.max).then_inc(fields_made, 1)
            v.tensor_copy(field[6][G], dst_i[G]).then_inc(fields_made, 1)

            dve.wait_ge(loaded_pair, 16)
            link(v.tensor_tensor(unsorted_at, pair[:, 0:REACH], pair[:, 1:REACH + 1], ALU.is_gt))
            v.tensor_reduce(small[:, 2:3], unsorted_at, AX.X, ALU.max).then_inc(first_row, 1)

            v.memset(slot_key[:, 0:1], 0)
            v.memset(rel_key[:, 0:1], 0)
            v.memset(win_key[:, 0:1], 255)
            v.memset(lane_key[:, 0:1], 0.0)
            v.memset(w_piece[:, 0:1, :], 0.0)
            v.memset(ones_col, 1.0)
            for f, to in enumerate((slot_key[:, 1:], lane_key[:, 1:], rel_key[:, 1:], win_key[:, 1:], src_idx, w_all, first_dst)):
                dve.wait_ge(field_t, f + 1)
                half = 4 * GROUP
                b = 2 * (f % 3)
                n = 1 if f == 6 else P
                v.tensor_copy(to[0:n, 0:half], psum[0:n, b, 0:half])
                link(v.tensor_copy(to[0:n, half:], psum[0:n, b + 1, 0:EDGE_TILES - half]))
                dve.sem_inc(field_out, 1)
            wp = w_piece[:, 1:, :]
            link(v.tensor_copy(wp[:, :, 0], w_all))
            link(v.tensor_tensor(w_rest, w_all, wp[:, :, 0], ALU.subtract))
            link(v.tensor_copy(wp[:, :, 1], w_rest))
            link(v.tensor_tensor(wp[:, :, 2], w_rest, wp[:, :, 1], ALU.subtract))
            dve.wait_ge(first_bc, 1)
            half = 4 * GROUP
            v.tensor_copy(first_all[:, 0:half], psum[:, 6, 0:half])
            link(v.tensor_copy(first_all[:, half:], psum[:, 7, 0:EDGE_TILES - half]))
            dve.wait_ge(pool_made, 5)
            for j in range(2):
                link(v.tensor_scalar(unsorted_at[:, 0:EDGE_TILES], first_all, small[:, j:j + 1], None, ALU.is_le))
                link(v.tensor_reduce(small[:, 4 + j:5 + j], unsorted_at[:, 0:EDGE_TILES], AX.X, ALU.add))
            dve.sem_inc(counts_made, 1)
            dve.wait_ge(flag_sum, 1)
            link(v.tensor_scalar(small[0:1, 8:9], psum[0:1, 5, 400:401], 0.5, None, ALU.is_lt))
            link(v.tensor_scalar(small[0:1, 9:10], small[0:1, 8:9], -1.0, 1.0, ALU.mult, ALU.add))
            dve.wait_ge(counts_out, 16)
            link(v.memset(row[0:1, 0, WINDOWS - 1:WINDOWS], float(EDGE_TILES)))
            link(v.tensor_scalar(row[0:1, 1, :], row[0:1, 0, :], 1.0, small[0:1, 8:9], ALU.max, ALU.mult))
            link(v.scalar_tensor_tensor(row[0:1, 2, :], row[0:1, 3, :], small[0:1, 9:10], row[0:1, 1, :], ALU.mult, ALU.add))
            v.tensor_copy(walk[0:1, 0:WINDOWS], row[0:1, 2, :])
            link(v.tensor_scalar(walk[0:1, WINDOWS:WINDOWS + 1], small[0:1, 9:10], float(EDGE_TILES), None, ALU.mult))
            dve.sem_inc(tables_ready, 1)
            dve.sem_inc(onehots_ready, 1)

            back = dve.value_load(walk[0:1, WINDOWS:WINDOWS + 1], min_val=0, max_val=EDGE_TILES)
            lo = dve.alloc_register("dve_lo")
            dve.reg_mov(lo, 0)
            col_reg = dve.alloc_register("dve_col")
            with dve.Fori(0, WINDOWS) as w:
                hi = dve.value_load(walk[0:1, ds(w, 1)], min_val=0, max_val=WINDOWS * EDGE_TILES)
                dve.wait_ge(onehots_ready, dve.snap(lo) + w + 1)
                v.tensor_scalar(in_window, win_key, iota_win[:, ds(w, 1)], None, ALU.is_equal).then_inc(masked, 1)
                dve.wait_ge(masked, w + 1)
                col0 = dve.snap(w * back)
                with dve.Fori(dve.snap(lo, min_val=0, max_val=WINDOWS * EDGE_TILES), hi) as c:
                    n = dve.snap(c + w)
                    dve.reg_mov(col_reg, c - col0 + 1)
                    col = dve.snap(col_reg, min_val=0, max_val=EDGE_TILES)
                    r = ring[:, ds(n & (ITEMS - 1), 1), :]
                    dve.wait_ge(items_done, n + 1)
                    m = in_window[:, ds(col, 1)]
                    v.tensor_scalar(r[:, :, 0:SLOT], iota_slot, slot_key[:, ds(col, 1)], m, ALU.is_equal, ALU.mult)
                    v.tensor_scalar(r[:, :, SLOT:SLOT + RCOL], iota_rel, rel_key[:, ds(col, 1)], m, ALU.is_equal, ALU.mult)
                    lane = lane_key[:, ds(col, 1)]
                    at = SLOT + RCOL
                    for k in range(3):
                        v.tensor_scalar(r[:, :, at + (k + 1) * P:at + (k + 2) * P], iota_lane, lane,
                                        w_piece[:, ds(col, 1), k], ALU.is_equal, ALU.mult)
                    v.tensor_scalar(r[:, :, at:at + P], iota_lane, lane, None, ALU.is_equal).then_inc(onehots_ready, 1)
                dve.reg_mov(lo, hi - 1)

        @block.tensor
        def _(pe):
            te = nc.tensor
            pe.wait_ge(pool_made, 5)
            pe.wait_ge(loaded_w, 3 * 16)
            for r in range(RELS):
                last = te.transpose(psum[:, 6 + r // 4, (r % 4) * P:(r % 4 + 1) * P], W_nat[:, r, :], ident0)
            last.then_inc(wt_done, 1)
            pe.wait_ge(wt_out, 1)
            for r in range(3):
                last = te.transpose(psum[:, 6, r * P:(r + 1) * P], W_nat[:, RELS + r, :], ident0)
            last.then_inc(wt_done, 1)
            for f in range(7):
                pe.wait_ge(fields_made, f + 1)
                source = field[f]
                if f >= 3:
                    pe.wait_ge(field_out, f - 2)
                b = 2 * (f % 3)
                for g in range(GROUPS):
                    last = te.transpose(psum[:, b + g // 4, (g % 4) * GROUP:(g % 4 + 1) * GROUP],
                                        source[0:GROUP, g, :], ident0[0:GROUP, 0:GROUP])
                last.then_inc(field_t, 1)
            pe.wait_ge(first_row, 1)
            pe.wait_ge(field_out, 6)
            te.matmul(psum[0:1, 5, 400:401], small[:, 2:3], ones[:, 0:1], start=True, stop=True).then_inc(flag_sum, 1)
            pe.wait_ge(field_out, 7)
            pe.wait_ge(wt_out, 2)
            half = 4 * GROUP
            te.matmul(psum[:, 6, 0:half], ones[0:1, :], first_dst[0:1, 0:half], start=True, stop=True)
            te.matmul(psum[:, 7, 0:EDGE_TILES - half], ones[0:1, :], first_dst[0:1, half:], start=True, stop=True).then_inc(first_bc, 1)

            pe.wait_ge(tables_ready, 1)
            pe.sem_inc(items_done, ITEMS)
            pe.sem_inc(rows_free, GSLOTS)
            back = pe.value_load(walk[0:1, WINDOWS:WINDOWS + 1], min_val=0, max_val=EDGE_TILES)
            lo = pe.alloc_register("pe_lo")
            pe.reg_mov(lo, 0)
            col_reg = pe.alloc_register("pe_col")
            at = SLOT + RCOL

            def item(c, w, col0, first):
                n = pe.snap(c + w)
                r = ring[:, ds(n & (ITEMS - 1), 1), :]
                g = grows[:, ds(c & (GSLOTS - 1), 1), :]
                bank = w & 1
                acc = psum[:, ds(bank * 4 + ACC, 1), 0:SLOT]
                wacc = psum[:, ds(bank * 4 + WACC, 1), 0:SLOT]
                racc = psum[:, ds(bank * 4 + RACC, 1), 0:RCOL]
                dacc = psum[0:3, ds(bank * 4 + RACC, 1), 256:256 + RCOL]
                pe.wait_ge(onehots_ready, n + 2)
                te.matmul(acc, r[:, :, at:at + P], r[:, :, 0:SLOT], start=first, stop=True, skip_group_check=True)
                for k in range(3):
                    te.matmul(wacc, r[:, :, at + (k + 1) * P:at + (k + 2) * P], r[:, :, 0:SLOT],
                              start=first and k == 0, stop=True, skip_group_check=True)
                pe.wait_ge(rows_ready, c + 1)
                rel = r[:, :, SLOT:SLOT + RCOL]
                for k in range(3):
                    ins = te.matmul(racc, g[:, :, k * FEAT:(k + 1) * FEAT], rel, start=first and k == 0, stop=True,
                                    skip_group_check=True)
                    if k == 0 and not first:
                        ins.then_inc(rows_free, 1)
                pe.reg_mov(col_reg, c - col0 + 1)
                col = pe.snap(col_reg, min_val=0, max_val=EDGE_TILES)
                te.matmul(dacc, w_piece[:, ds(col, 1), :], rel, start=False, stop=True,
                          skip_group_check=True).then_inc(items_done, 1)

            with pe.Fori(0, BLOCKS) as b:
                with pe.Fori(b * (P // WIN), (b + 1) * (P // WIN)) as w:
                    hi = pe.value_load(walk[0:1, ds(w, 1)], min_val=0, max_val=WINDOWS * EDGE_TILES)
                    start = pe.snap(lo, min_val=0, max_val=WINDOWS * EDGE_TILES)
                    col0 = pe.snap(w * back)
                    pe.wait_ge(acc_free, w + 1)
                    item(start, w, col0, True)
                    with pe.If(start + 1 < hi):
                        with pe.Fori(start + 1, hi) as c:
                            item(c, w, col0, False)
                    pe.reg_mov(lo, hi - 1)
                pe.wait_ge(acc_free, (b + 1) * (P // WIN) + 2)
                blk = ds((b & 1) * 4 + BLK, 1)
                for r in range(RELS):
                    te.matmul(psum[:, blk, 0:FEAT], rel_sum[:, r, :], WrelT[:, r, :], start=r == 0, stop=True,
                              skip_group_check=True)
                for r in range(RELS):
                    last = te.matmul(psum[:, blk, FEAT:FEAT + 1], deg_sum[0:3, r, :], ones_col[0:3, :], start=False,
                                     stop=True, skip_group_check=True)
                last.then_inc(rel_ready, 1)

        @block.scalar
        def _(act):
            sc = nc.scalar
            act.wait_ge(zeroed, 1)
            last_rows = (BLOCKS - 1) * P
            act.dma_start(x_nat[:, 0:BLOCKS - 1, :], x[0:last_rows, :].rearrange("(h p) f -> p h f", p=P)).then_inc(loaded_x, 16)
            act.dma_start(x_nat[0:TAIL, BLOCKS - 1, :], x[last_rows:NODES, :]).then_inc(loaded_x, 16)
            act.dma_start(pair, bass.AP(dst.tensor, dst.offset, [[SPAN, P], [1, REACH + 1]])).then_inc(loaded_pair, 16)
            act.dma_start(W_nat[:, 0:RELS, :], W_rel.rearrange("r o f -> o r f")).then_inc(loaded_w, 16)
            act.dma_start(W_nat[:, RELS:RELS + 2, :], W_sum.rearrange("o (a f) -> o a f", a=2)).then_inc(loaded_w, 16)
            act.dma_start(W_nat[:, RELS + 2, :], W_deg).then_inc(loaded_w, 16)
            act.wait_ge(wt_done, 1)
            for h in range(2):
                last = sc.activation(WrelT[:, 4 * h:4 * h + 4, :].rearrange("p a b -> p (a b)"), psum[:, 6 + h, 0:512], ACT.Copy)
            last.then_inc(wt_out, 1)
            act.wait_ge(wt_done, 2)
            sc.activation(W_t.rearrange("p a b -> p (a b)"), psum[:, 6, 0:3 * P], ACT.Copy).then_inc(wt_out, 1)

            act.wait_ge(tables_ready, 1)
            act.sem_inc(acc_free, 2)

            def one_block(b, first_block):
                for q in range(4):
                    stage = q % 2
                    for k in range(2):
                        j = 2 * q + k
                        w = act.snap(b * (P // WIN) + j)
                        hi = act.value_load(walk[0:1, ds(w, 1)], min_val=0, max_val=WINDOWS * EDGE_TILES)
                        bank = (j & 1) * 4
                        act.wait_ge(items_done, hi + w + ITEMS)
                        sc.activation(adj[:, :, ds(w * WIN, WIN)],
                                      psum[:, bank + ACC, 0:SLOT].rearrange("p (h r) -> p h r", r=WIN), ACT.Copy)
                        if k == 0 and not (first_block and q < 2):
                            act.wait_ge(wadj_stored[stage], (b * 2 + (q // 2)) * 16)
                        sc.activation(wstage[:, stage, :, k * WIN:(k + 1) * WIN],
                                      psum[:, bank + WACC, 0:SLOT].rearrange("p (h r) -> p h r", r=WIN), ACT.Copy)
                        sc.activation(rel_sum[:, :, j * WIN:(j + 1) * WIN],
                                      psum[:, bank + RACC, 0:RCOL].rearrange("p (t r) -> p t r", r=WIN), ACT.Copy)
                        sc.activation(deg_sum[0:3, :, j * WIN:(j + 1) * WIN],
                                      psum[0:3, bank + RACC, 256:256 + RCOL].rearrange("p (t r) -> p t r", r=WIN),
                                      ACT.Copy).then_inc(acc_free, 1)
                    act.wait_ge(acc_free, b * (P // WIN) + (2 * q + 4))
                    act.dma_start(wadj[ds(b * 4 + q, 1), :, :].rearrange("o p c -> p (o c)"),
                                  wstage[:, stage, :, :].rearrange("p h r -> p (h r)")).then_inc(wadj_stored[stage], 16)
                act.wait_ge(rel_ready, b + 1)
                if not first_block:
                    act.wait_ge(rel_stored, b * 16)
                sc.activation(rel_row, psum[:, ds((b & 1) * 4 + BLK, 1), 0:FEAT + 1], ACT.Copy).then_inc(rel_evac, 1)
                act.wait_ge(rel_evac, b + 1)
                act.dma_start(rel_out[ds(b * P, P), :], rel_row).then_inc(rel_stored, 16)

            one_block(0, True)
            with act.Fori(1, BLOCKS) as b:
                one_block(b, False)
            for s in wadj_stored:
                act.wait_ge(s, 2 * BLOCKS * 16)
            act.wait_ge(rel_stored, BLOCKS * 16)

        block.__exit__(None, None, None)

        def split(v, link, pieces, value, rest):
            link(v.tensor_copy(pieces[:, 0:FEAT], value))
            link(v.tensor_tensor(rest, value, pieces[:, 0:FEAT], ALU.subtract))
            link(v.tensor_copy(pieces[:, FEAT:2 * FEAT], rest))
            link(v.tensor_tensor(pieces[:, 2 * FEAT:3 * FEAT], rest, pieces[:, FEAT:2 * FEAT], ALU.subtract))

        def each_block(engine, step):
            with engine.Fori(0, BLOCKS // 2) as j:
                step(engine.snap(j * 2), 0)
                step(engine.snap(j * 2 + 1), 1)
            step(BLOCKS - 1, 0)

        def each_block_ahead(engine, ahead, step):
            ahead(0, 0)
            with engine.Fori(0, BLOCKS // 2) as j:
                ahead(engine.snap(j * 2 + 1), 1)
                step(engine.snap(j * 2), 0)
                ahead(engine.snap(j * 2 + 2), 0)
                step(engine.snap(j * 2 + 1), 1)
            step(BLOCKS - 1, 0)

        PIECES = 3 * FEAT + 2
        cut = cutter(work_mem, 0, WORK_BYTES)
        pieces_a = cut([BLOCKS, PIECES], bf16)
        x_now = cut([BLOCKS, FEAT], f32)
        side = cut([BLOCKS, FEAT], f32)
        ident = cut([P], f32)
        W_now = cut([2 * FEAT], f32)
        W_next = cut([FEAT], f32)
        bias_now = cut([FEAT], f32)
        bias_next = cut([FEAT], f32)
        u = cut([2, FEAT], f32)
        uT = cut([2, FEAT], f32)
        tmp = cut([FEAT], f32)
        rest = cut([FEAT], f32)
        stats = cut([BLOCKS, 6], f32)
        moments = cut([BLOCKS, 2], f32)
        spread = cut([BLOCKS], f32)
        dinv_w = cut([BLOCKS], f32)
        dinv_c = cut([BLOCKS], f32)
        eps_col = cut([2], f32)
        rows_full = (BLOCKS - 1) * P

        loaded, c_ready, pad_zero = sem("l1_loaded"), sem("l1_const"), sem("l1_pad_zero")
        step1, var_ready, std_ready = sem("l1_step"), sem("l1_var"), sem("l1_std")
        a_u, a_t, a_ut, a_keep, a_h, a_free = (sem("l1a_" + n) for n in ("u", "t", "ut", "keep", "h", "hfree"))
        b_s, b_sfree, b_var, b_std, b_u, b_t, b_ut, b_keep, b_h, b_hfree = (
            sem("l1b_" + n) for n in ("s", "sfree", "var", "std", "u", "t", "ut", "keep", "h", "hfree"))
        with nc.Block() as block:
            @block.sync
            def _(sp):
                sp.wait_ge(pad_zero, 1)
                sp.dma_start(x_now[:, 0:BLOCKS - 1, :], x[0:rows_full, :].rearrange("(h p) f -> p h f", p=P)).then_inc(loaded, 16)
                sp.dma_start(x_now[0:TAIL, BLOCKS - 1, :], x[rows_full:NODES, :]).then_inc(loaded, 16)
                rel = rel_out.rearrange("(h p) f -> p h f", p=P)
                sp.dma_start(side, rel[:, :, 0:FEAT]).then_inc(loaded, 16)
                sp.dma_start(dinv_w.rearrange("p (h o) -> p h o", o=1), rel[:, :, FEAT:FEAT + 1],
                             allow_slow_non_contiguous=True).then_inc(loaded, 16)
                sp.dma_start(W_now, weights_t[:, 0:2 * FEAT]).then_inc(loaded, 16)
                sp.dma_start(W_next, weights_t[:, 2 * FEAT:3 * FEAT]).then_inc(loaded, 16)
                for to, t in ((bias_now, b_sum), (bias_next, b_deg)):
                    sp.dma_start(to, bass.AP(t.tensor, t.offset, [[0, P], [1, FEAT]])).then_inc(loaded, 16)

            @block.gpsimd
            def _(pool):
                nc.gpsimd.memset(uT[:, 0, :], 1.0).then_inc(c_ready, 1)
                pool.wait_ge(c_ready, 1)
                nc.gpsimd.affine_select(out=ident, in_=uT[:, 0, :], compare_op=ALU.is_equal, fill=0.0, base=0,
                                        pattern=[[-1, P]], channel_multiplier=1).then_inc(c_ready, 1)
                nc.gpsimd.memset(pieces_a[:, :, 3 * FEAT:PIECES], 1.0).then_inc(c_ready, 1)
                nc.gpsimd.memset(eps_col[:, 0:1], EPS).then_inc(c_ready, 1)
                nc.gpsimd.memset(eps_col[:, 1:2], 1.0).then_inc(c_ready, 1)

            @block.vector
            def _(dve):
                v = nc.vector
                linked = dve.alloc_register("l1_linked")
                dve.reg_mov(linked, 0)

                def link(ins):
                    ins.then_inc(step1, 1)
                    dve.wait_ge(step1, dve.snap(linked) + 1)
                    dve.reg_add(linked, linked, 1)

                v.memset(x_now[:, BLOCKS - 1, :], 0.0).then_inc(pad_zero, 1)
                dve.wait_ge(loaded, 8 * 16)
                link(v.tensor_tensor(x_now, x_now, side, ALU.add))
                for b in range(BLOCKS):
                    last = v.bn_stats(stats[:, b, :], x_now[:, b, :])
                link(last)
                for b in range(BLOCKS):
                    last = v.bn_aggr(moments[:, b, :], stats[:, b, :])
                last.then_inc(var_ready, 1)
                dve.wait_ge(std_ready, 2)
                link(v.reciprocal(spread, spread))
                link(v.reciprocal(dinv_w, dinv_w))
                dve.sem_inc(a_keep, 2)

                def normalise(b, s):
                    dve.wait_ge(a_keep, b + 1)
                    v.tensor_scalar(u[:, s, :], x_now[:, ds(b, 1), :], moments[:, ds(b, 1), 0], spread[:, ds(b, 1)],
                                    ALU.subtract, ALU.mult).then_inc(a_u, 1)

                def take_products(b, s):
                    dve.wait_ge(a_h, b + 1)
                    h = psum[:, 2 + s, :]
                    v.tensor_tensor(side[:, ds(b, 1), :], h[:, 0:FEAT], bias_now, ALU.add)
                    split(v, link, pieces_a[:, ds(b, 1), :].rearrange("p o c -> p (o c)"), h[:, FEAT:2 * FEAT], rest)
                    dve.sem_inc(a_free, 1)

                each_block_ahead(dve, normalise, take_products)

                def layer1(b, s):
                    dve.wait_ge(b_s, b + 1)
                    agg = psum[:, s, :]
                    link(v.tensor_tensor(tmp, agg[:, 0:FEAT], side[:, ds(b, 1), :], ALU.add))
                    link(v.tensor_tensor(tmp, agg[:, FEAT:2 * FEAT], tmp, ALU.add))
                    link(v.tensor_tensor(tmp, agg[:, 2 * FEAT:3 * FEAT], tmp, ALU.add))
                    v.tensor_scalar(dinv_c[:, ds(b, 1)], agg[:, 3 * FEAT:3 * FEAT + 1], 1.0, None, ALU.max).then_inc(b_sfree, 1)
                    link(v.scalar_tensor_tensor(tmp, tmp, 0.0, x_now[:, ds(b, 1), :], ALU.max, ALU.add))
                    link(v.bn_stats(stats[:, s, :], tmp))
                    v.bn_aggr(moments[:, s, :], stats[:, s, :]).then_inc(b_var, 1)
                    dve.wait_ge(b_std, b + 1)
                    link(v.reciprocal(spread[:, s:s + 1], spread[:, s:s + 1]))
                    dve.wait_ge(b_keep, b + 1)
                    v.tensor_scalar(u[:, s, :], tmp, moments[:, s, 0:1], spread[:, s:s + 1],
                                    ALU.subtract, ALU.mult).then_inc(b_u, 1)
                    dve.wait_ge(b_h, b + 1)
                    link(v.tensor_tensor(tmp, psum[:, 4 + s, 0:FEAT], bias_next, ALU.add))
                    link(v.tensor_scalar(side[:, ds(b, 1), :], tmp, dinv_w[:, ds(b, 1)], None, ALU.mult))
                    dve.sem_inc(b_hfree, 1)

                dve.wait_ge(a_keep, BLOCKS + 2)
                dve.sem_inc(b_keep, 2)
                each_block(dve, layer1)

            @block.scalar
            def _(act):
                sc = nc.scalar
                act.wait_ge(c_ready, 5)
                act.wait_ge(var_ready, 1)
                sc.activation(spread, moments[:, :, 1], ACT.Sqrt, bias=eps_col[:, 0:1]).then_inc(std_ready, 1)
                sc.activation(dinv_w, dinv_w, ACT.Sqrt, bias=eps_col[:, 1:2]).then_inc(std_ready, 1)

                def turn(b, s):
                    act.wait_ge(a_t, b + 1)
                    sc.activation(uT[:, s, :], psum[:, s, 0:P], ACT.Copy).then_inc(a_ut, 1)
                    sc.activation(x_now[:, ds(b, 1), :], u[:, s, :], ACT.Copy).then_inc(a_keep, 1)

                each_block(act, turn)

                def layer1(b, s):
                    act.wait_ge(b_var, b + 1)
                    sc.activation(spread[:, s:s + 1], moments[:, s, 1:2], ACT.Sqrt, bias=eps_col[:, 0:1]).then_inc(b_std, 1)
                    act.wait_ge(b_t, b + 1)
                    sc.activation(uT[:, s, :], psum[:, 2 + s, 0:P], ACT.Copy).then_inc(b_ut, 1)
                    sc.activation(x_now[:, ds(b, 1), :], u[:, s, :], ACT.Copy).then_inc(b_keep, 1)

                each_block(act, layer1)

            @block.tensor
            def _(pe):
                te = nc.tensor
                pe.wait_ge(c_ready, 3)
                pe.sem_inc(a_free, 2)
                pe.sem_inc(b_sfree, 2)
                pe.sem_inc(b_hfree, 2)

                def turn(b, s):
                    pe.wait_ge(a_u, b + 1)
                    te.transpose(psum[:, s, 0:P], u[:, s, :], ident).then_inc(a_t, 1)

                def product(b, s):
                    pe.wait_ge(a_ut, b + 1)
                    pe.wait_ge(a_free, b + 1)
                    te.matmul(psum[:, 2 + s, 0:2 * FEAT], uT[:, s, :], W_now, start=True, stop=True).then_inc(a_h, 1)

                each_block_ahead(pe, turn, product)

                def aggregate(b, s):
                    pe.wait_ge(b_sfree, b + 1)
                    for h in range(BLOCKS):
                        last = te.matmul(psum[:, s, 0:3 * FEAT + 1], adj[:, h, ds(b * P, P)], pieces_a[:, h, 0:3 * FEAT + 1],
                                         start=h == 0, stop=h == BLOCKS - 1)
                    last.then_inc(b_s, 1)

                def next_product(b, s):
                    pe.wait_ge(b_u, b + 1)
                    te.transpose(psum[:, 2 + s, 0:P], u[:, s, :], ident).then_inc(b_t, 1)
                    pe.wait_ge(b_ut, b + 1)
                    pe.wait_ge(b_hfree, b + 1)
                    te.matmul(psum[:, 4 + s, 0:FEAT], uT[:, s, :], W_next, start=True, stop=True).then_inc(b_h, 1)

                pe.wait_ge(a_free, BLOCKS + 2)
                each_block_ahead(pe, aggregate, next_product)

        CHUNK = 5
        CHUNKS = BLOCKS // CHUNK
        PER = P // QUARTER
        cut = cutter(work_mem, 0, BLOCKS * PIECES * 2)
        wchunk = cut([CHUNKS, PER, CHUNK * QUARTER], f32)
        gamma_all, beta_all = cut([FEAT], f32), cut([FEAT], f32)
        W_first = cut([FEAT], f32)
        first_pieces = cut([2, 3 * FEAT], bf16)
        first_sum = cut([2, FEAT], f32)
        aggT = cut([2, P], f32)
        agg_free, turned, turned_free = sem("l2_agg_free"), sem("l2_turned"), sem("l2_turned_free")
        loaded, step2 = sem("l2_loaded"), sem("l2_step")
        chunk_landed = [sem(f"l2_chunk{i}") for i in range(CHUNKS)]
        chunk_free, s_done, var, std, u_ready, u_t, ut_ready, u_free, h_done, sum_ready, split_ready, out_free, stored, cnt = (
            sem("l2_" + n) for n in ("chunk_free", "s", "var", "std", "u", "t", "ut", "ufree", "h", "sum",
                                     "split", "outfree", "stored", "cnt"))
        with nc.Block() as block:
            @block.sync
            def _(sp):
                for to, t in ((gamma_all, gamma), (beta_all, beta)):
                    sp.dma_start(to, bass.AP(t.tensor, t.offset, [[0, P], [1, FEAT]])).then_inc(loaded, 16)
                sp.dma_start(W_first, W_cheb[0, :, :]).then_inc(loaded, 16)
                wq = wadj.rearrange("q p (h r) -> q p h r", h=BLOCKS)
                with sp.Fori(0, BLOCKS) as b:
                    for c in range(CHUNKS):
                        sp.wait_ge(chunk_free, b * CHUNKS + (c + 1))
                        sp.dma_start(wchunk[:, c, :, :],
                                     wq[ds(b * PER, PER), :, c * CHUNK:(c + 1) * CHUNK, :].rearrange("q p h r -> p q (h r)")
                                     ).then_inc(chunk_landed[c], 16)

            @block.gpsimd
            def _(pool):
                def store(b, s):
                    rows = ds(b * P, P)
                    pool.wait_ge(split_ready, b + 1)
                    pool.wait_ge(sum_ready, b + 1)
                    pool.reg_mov(at, b + 0)
                    nc.gpsimd.dma_start(cheb_prev[0, rows, :], u[:, s, :]).then_inc(stored, 16)
                    nc.gpsimd.dma_start(u_pieces[rows, :], first_pieces[:, s, :]).then_inc(stored, 16)
                    nc.gpsimd.dma_start(cheb_sum[rows, :], first_sum[:, s, :]).then_inc(stored, 16)
                    pool.wait_ge(stored, b * 48 + 48)
                    pool.sem_inc(out_free, 1)

                at = pool.alloc_register("l2_at")
                pool.sem_inc(out_free, 2)
                each_block(pool, store)

            @block.vector
            def _(dve):
                v = nc.vector
                linked = dve.alloc_register("l2_linked")
                dve.reg_mov(linked, 0)

                def link(ins):
                    ins.then_inc(step2, 1)
                    dve.wait_ge(step2, dve.snap(linked) + 1)
                    dve.reg_add(linked, linked, 1)

                dve.wait_ge(loaded, 48)
                dve.wait_ge(cnt, 1)
                link(v.reciprocal(dinv_c, dinv_c))

                def layer2(b, s):
                    one = ds(b, 1)

                    def norm_stats(n):
                        link(v.bn_stats(stats[:, s, :], tmp))
                        v.bn_aggr(moments[:, s, :], stats[:, s, :]).then_inc(var, 1)
                        dve.wait_ge(std, b * 2 + n)
                        link(v.reciprocal(spread[:, s:s + 1], spread[:, s:s + 1]))

                    dve.wait_ge(turned, b + 1)
                    link(v.tensor_tensor(tmp, psum[:, 6 + s, 0:FEAT], side[:, one, :], ALU.add))
                    dve.sem_inc(turned_free, 1)
                    link(v.tensor_scalar(tmp, tmp, dinv_w[:, one], None, ALU.mult))
                    link(v.scalar_tensor_tensor(tmp, tmp, SLOPE, tmp, ALU.mult, ALU.max))
                    norm_stats(1)
                    link(v.tensor_scalar(tmp, tmp, moments[:, s, 0:1], spread[:, s:s + 1], ALU.subtract, ALU.mult))
                    link(v.tensor_tensor(tmp, tmp, gamma_all, ALU.mult))
                    link(v.tensor_tensor(tmp, tmp, beta_all, ALU.add))
                    link(v.tensor_tensor(tmp, tmp, x_now[:, one, :], ALU.add))
                    norm_stats(2)
                    dve.wait_ge(out_free, b + 1)
                    dve.wait_ge(u_free, b + 1)
                    link(v.tensor_scalar(u[:, s, :], tmp, moments[:, s, 0:1], spread[:, s:s + 1], ALU.subtract, ALU.mult))
                    dve.sem_inc(u_ready, 1)
                    link(v.tensor_scalar(tmp, u[:, s, :], dinv_c[:, one], None, ALU.mult))
                    split(v, link, first_pieces[:, s, :], tmp, rest)
                    dve.sem_inc(split_ready, 1)

                each_block(dve, layer2)

            @block.scalar
            def _(act):
                sc = nc.scalar
                sc.activation(dinv_c, dinv_c, ACT.Sqrt).then_inc(cnt, 1)
                act.sem_inc(u_free, 2)

                def turn(b, s):
                    act.wait_ge(s_done, b + 1)
                    sc.activation(aggT[:, s, :], psum[:, s, 0:P], ACT.Copy).then_inc(agg_free, 1)
                    for n in range(2):
                        act.wait_ge(var, b * 2 + (n + 1))
                        sc.activation(spread[:, s:s + 1], moments[:, s, 1:2], ACT.Sqrt, bias=eps_col[:, 0:1]).then_inc(std, 1)
                    act.wait_ge(u_t, b + 1)
                    sc.activation(uT[:, s, :], psum[:, 2 + s, 0:P], ACT.Copy).then_inc(ut_ready, 1)
                    act.sem_inc(u_free, 1)
                    act.wait_ge(h_done, b + 1)
                    act.wait_ge(out_free, b + 1)
                    sc.activation(first_sum[:, s, :], psum[:, 4 + s, 0:FEAT], ACT.Copy).then_inc(sum_ready, 1)

                each_block(act, turn)

            @block.tensor
            def _(pe):
                te = nc.tensor
                pe.sem_inc(chunk_free, CHUNKS)
                pe.sem_inc(agg_free, 1)
                pe.sem_inc(turned_free, 2)
                pe.wait_ge(loaded, 48)

                def turn_back(b, s):
                    pe.wait_ge(agg_free, b + 2)
                    pe.wait_ge(turned_free, b + 1)
                    te.transpose(psum[:, 6 + s, 0:P], aggT[:, s, :], ident).then_inc(turned, 1)

                def aggregate(b, s, first=False):
                    for c in range(CHUNKS):
                        pe.wait_ge(chunk_landed[c], b * 16 + 16)
                        for i in range(CHUNK):
                            h = c * CHUNK + i
                            last = te.matmul(psum[:, s, 0:P], side[:, h, :],
                                             wchunk[:, c, :, i * QUARTER:(i + 1) * QUARTER],
                                             start=h == 0, stop=h == BLOCKS - 1, skip_group_check=True)
                        if c < CHUNKS - 1:
                            last.then_inc(chunk_free, 1)
                        else:
                            last.then_inc(s_done, 1)
                        if c == 1 and not first:
                            turn_back(b - 1, 1 - s)
                    pe.wait_ge(s_done, b + 1)
                    pe.sem_inc(chunk_free, 1)

                def product(b, s):
                    pe.wait_ge(u_ready, b + 1)
                    te.transpose(psum[:, 2 + s, 0:P], u[:, s, :], ident).then_inc(u_t, 1)
                    pe.wait_ge(ut_ready, b + 1)
                    te.matmul(psum[:, 4 + s, 0:FEAT], uT[:, s, :], W_first, start=True, stop=True).then_inc(h_done, 1)

                aggregate(0, 0, True)
                with pe.Fori(0, BLOCKS // 2) as j:
                    aggregate(pe.snap(j * 2 + 1), 1)
                    product(pe.snap(j * 2), 0)
                    aggregate(pe.snap(j * 2 + 2), 0)
                    product(pe.snap(j * 2 + 1), 1)
                turn_back(BLOCKS - 1, 0)
                product(BLOCKS - 1, 0)

        cut = cutter(work_mem, BLOCKS * PIECES, WORK_BYTES)
        pieces_b = cut([BLOCKS, PIECES], bf16)
        prev = cut([2, FEAT], f32)
        sum_in = cut([2, FEAT], f32)
        res_in = cut([2, FEAT], f32)
        sum_out = cut([2, FEAT], f32)

        def cheb_step(k, pieces, pieces_next):
            name = f"c{k}_"
            (loaded, stepk, s_done, s_free, u_ready, u_t, ut_ready, u_free, h_done, in_free, var, std, sum_ready, out_free,
             stored) = (sem(name + n) for n in ("loaded", "step", "s", "sfree", "u", "t", "ut", "ufree", "h", "infree",
                                                "var", "std", "sum", "outfree", "stored"))
            tiles_landed = [sem(name + f"tiles{i}") for i in range(2)]
            loads = [(sum_in, cheb_sum)]
            if k > 1:
                loads.append((prev, cheb_prev[k - 2]))
            if k == 3:
                loads.append((res_in, cheb_prev[0]))
            with nc.Block() as block:
                @block.sync
                def _(sp):
                    sp.dma_start(W_next, W_cheb[k, :, :]).then_inc(loaded, 16)
                    if k == 1:
                        sp.dma_start(pieces[:, :, 0:3 * FEAT], u_pieces.rearrange("(h p) c -> p h c", p=P)).then_inc(loaded, 16)

                    def load(b, s):
                        sp.wait_ge(in_free, b + 1)
                        for to, source in loads:
                            sp.dma_start(to[:, s, :], source[ds(b * P, P), :]).then_inc(tiles_landed[s], 16)

                    each_block(sp, load)

                @block.gpsimd
                def _(pool):
                    at = pool.alloc_register(name + "at")
                    pool.sem_inc(out_free, 2)
                    n = 2 if k == 1 else 1

                    def store(b, s):
                        pool.wait_ge(sum_ready, b + 1)
                        pool.reg_mov(at, b + 0)
                        if k == 3:
                            if isinstance(b, int):
                                nc.gpsimd.dma_start(out[rows_full:NODES, :], sum_out[0:TAIL, s, :]).then_inc(stored, 16)
                            else:
                                nc.gpsimd.dma_start(out[ds(b * P, P), :], sum_out[:, s, :]).then_inc(stored, 16)
                        else:
                            nc.gpsimd.dma_start(cheb_sum[ds(b * P, P), :], sum_out[:, s, :]).then_inc(stored, 16)
                            if k == 1:
                                nc.gpsimd.dma_start(cheb_prev[1, ds(b * P, P), :], u[:, s, :]).then_inc(stored, 16)
                        pool.wait_ge(stored, b * (16 * n) + 16 * n)
                        pool.sem_inc(out_free, 1)

                    each_block(pool, store)

                @block.vector
                def _(dve):
                    v = nc.vector
                    linked = dve.alloc_register(name + "linked")
                    dve.reg_mov(linked, 0)
                    dve.sem_inc(in_free, 2)

                    def link(ins):
                        ins.then_inc(stepk, 1)
                        dve.wait_ge(stepk, dve.snap(linked) + 1)
                        dve.reg_add(linked, linked, 1)

                    def step(b, s):
                        one = ds(b, 1)
                        nl = len(loads)
                        dve.wait_ge(s_done, b + 1)
                        link(v.tensor_copy(tmp, psum[:, s, 0:FEAT]))
                        link(v.tensor_tensor(tmp, psum[:, s, FEAT:2 * FEAT], tmp, ALU.add))
                        link(v.tensor_tensor(tmp, psum[:, s, 2 * FEAT:3 * FEAT], tmp, ALU.add))
                        dve.sem_inc(s_free, 1)
                        link(v.tensor_scalar(tmp, tmp, dinv_c[:, one], 1.0 if k == 1 else 2.0, ALU.mult, ALU.mult))
                        dve.wait_ge(tiles_landed[s], (b - s) * (8 * nl) + 16 * nl)
                        dve.wait_ge(out_free, b + 1)
                        dve.wait_ge(u_free, b + 1)
                        if k == 1:
                            link(v.tensor_copy(u[:, s, :], tmp))
                        else:
                            link(v.tensor_tensor(u[:, s, :], tmp, prev[:, s, :], ALU.subtract))
                        dve.sem_inc(u_ready, 1)
                        if k < 3:
                            link(v.tensor_scalar(tmp, u[:, s, :], dinv_c[:, one], None, ALU.mult))
                            split(v, link, pieces_next[:, one, :].rearrange("p o c -> p (o c)"), tmp, rest)
                        dve.wait_ge(h_done, b + 1)
                        if k < 3:
                            link(v.tensor_tensor(sum_out[:, s, :], psum[:, 4 + s, 0:FEAT], sum_in[:, s, :], ALU.add))
                        else:
                            link(v.tensor_tensor(tmp, psum[:, 4 + s, 0:FEAT], sum_in[:, s, :], ALU.add))
                            link(v.tensor_tensor(tmp, tmp, res_in[:, s, :], ALU.add))
                            link(v.bn_stats(stats[:, s, :], tmp))
                            v.bn_aggr(moments[:, s, :], stats[:, s, :]).then_inc(var, 1)
                            dve.wait_ge(std, b + 1)
                            link(v.reciprocal(spread[:, s:s + 1], spread[:, s:s + 1]))
                            link(v.tensor_scalar(sum_out[:, s, :], tmp, moments[:, s, 0:1], spread[:, s:s + 1],
                                                 ALU.subtract, ALU.mult))
                        dve.sem_inc(sum_ready, 1)
                        dve.sem_inc(in_free, 1)

                    each_block(dve, step)

                @block.scalar
                def _(act):
                    act.sem_inc(u_free, 2)

                    def turn(b, s):
                        act.wait_ge(u_t, b + 1)
                        nc.scalar.activation(uT[:, s, :], psum[:, 2 + s, 0:P], ACT.Copy).then_inc(ut_ready, 1)
                        act.sem_inc(u_free, 1)
                        if k == 3:
                            act.wait_ge(var, b + 1)
                            nc.scalar.activation(spread[:, s:s + 1], moments[:, s, 1:2], ACT.Sqrt,
                                                 bias=eps_col[:, 0:1]).then_inc(std, 1)

                    each_block(act, turn)

                @block.tensor
                def _(pe):
                    te = nc.tensor
                    pe.sem_inc(s_free, 2)
                    pe.wait_ge(loaded, 32 if k == 1 else 16)

                    def aggregate(b, s):
                        pe.wait_ge(s_free, b + 1)
                        for h in range(BLOCKS):
                            last = te.matmul(psum[:, s, 0:3 * FEAT], adj[:, h, ds(b * P, P)], pieces[:, h, 0:3 * FEAT],
                                             start=h == 0, stop=h == BLOCKS - 1)
                        last.then_inc(s_done, 1)

                    def product(b, s):
                        pe.wait_ge(u_ready, b + 1)
                        te.transpose(psum[:, 2 + s, 0:P], u[:, s, :], ident).then_inc(u_t, 1)
                        pe.wait_ge(ut_ready, b + 1)
                        te.matmul(psum[:, 4 + s, 0:FEAT], uT[:, s, :], W_next, start=True, stop=True).then_inc(h_done, 1)

                    each_block_ahead(pe, aggregate, product)

        cheb_step(1, pieces_a, pieces_b)
        cheb_step(2, pieces_b, pieces_a)
        cheb_step(3, pieces_a, None)


_INS = ["x", "src", "dst", "edge_attr_4", "edge_type_8", "L0_gnn_W", "L1_gnn_W", "L1_gnn_b", "L2_gnn_W", "L2_gnn_b",
        "L2_gnn_gamma", "L2_gnn_beta", "L3_gnn_weights"]


def kernel(**inputs):
    import numpy as np
    import concourse.bacc as bacc
    from concourse.bass_utils import run_bass_kernel_spmd

    nc = bacc.Bacc("TRN2", target_bir_lowering=False, num_devices=1)
    arrays, args = {}, []
    for name in _INS:
        a = np.ascontiguousarray(inputs[name])
        arrays[f"in_{name}"] = a
        args.append(nc.dram_tensor(f"in_{name}", a.shape, mybir.dt.from_np(a.dtype), kind="ExternalInput").ap())
    args.append(nc.dram_tensor("out_x", (NODES, FEAT), mybir.dt.float32, kind="ExternalOutput").ap())
    gnn_kernel(nc, *args)
    r = run_bass_kernel_spmd(nc, [arrays], core_ids=[0])
    return r.results[0]["out_x"]
```
